# Optimizing a Trainium2 kernel written in Bass

```python
import numpy as np
import jax
import jax.numpy as jnp

def _softmax(x, axis=-1):
    return jax.nn.softmax(x, axis=axis)

def _gelu(x):
    return jax.nn.gelu(x, approximate=True)

def _silu(x):
    return jax.nn.silu(x)

def _sigmoid(x):
    return jax.nn.sigmoid(x)

def _layernorm(x, axis=-1, eps=1e-05):
    m = jnp.mean(x, axis=axis, keepdims=True)
    v = jnp.var(x, axis=axis, keepdims=True)
    return (x - m) / jnp.sqrt(v + eps)

def _scatter_add(tgt, idx, src, axis=0):
    return tgt.at[idx].add(src)

def _segment_sum(src, seg, n):
    return jax.ops.segment_sum(src, seg, n)
kernel_name = 'mk_gps_d1_gnn_r8_decd07'

def setup_inputs(seed: int=0):
    np.random.seed(seed)
    _w = jnp.asarray

    def _rec_inputs():
        import jax
        import jax.numpy as jnp
        _gk = jax.random.key(seed)
        x = -0.0003713 + 1 * jax.random.normal(jax.random.fold_in(_gk, 1), (6250, 256), jnp.float32)
        src = jax.random.randint(jax.random.fold_in(_gk, 2), (200000,), 0, 6250, jnp.int32)
        dst = jax.random.randint(jax.random.fold_in(_gk, 3), (200000,), 0, 6250, jnp.int32)
        _o = jnp.argsort(dst, stable=True)
        src = src[_o]
        dst = dst[_o]
        return (x, src, dst)
    x, src, dst = _rec_inputs()

    def _L0_gnn_setup():
        import jax, jax.numpy as jnp
        import numpy as np
        N_NODES = 6250
        N_EDGES = 100000
        IN_SIZE = 256
        OUT_SIZE = 256
        key = jax.random.key(seed)
        k1, k2, k3, k4, k5 = jax.random.split(key, 5)
        x = jax.random.normal(k1, (N_NODES, IN_SIZE), dtype=jnp.float32)
        bound = 1.0 / np.sqrt(IN_SIZE)
        W = jax.random.uniform(k2, (IN_SIZE, OUT_SIZE), minval=-bound, maxval=bound, dtype=jnp.float32)
        b = jax.random.uniform(k3, (OUT_SIZE,), minval=-bound, maxval=bound, dtype=jnp.float32)
        edge_src = jax.random.randint(k4, (N_EDGES,), 0, N_NODES, dtype=jnp.int32)
        edge_dst = jax.random.randint(k5, (N_EDGES,), 0, N_NODES, dtype=jnp.int32)
        return {'x': x, 'W': W, 'b': b, 'edge_src': edge_src, 'edge_dst': edge_dst}
    _L0_gnn_all = _L0_gnn_setup()
    _L0_gnn_in = {k: v for k, v in _L0_gnn_all.items() if k in ('W', 'b')}
    del _L0_gnn_all

    def _L0_mix_setup():
        import jax, jax.numpy as jnp
        import numpy as np
        B, N, C = (8, 1024, 256)
        HEADS, DH, KR = (8, 32, 4)
        INNER = HEADS * DH
        FF = 4 * C
        EPS = 1e-05

        def layernorm(x, g, b):
            mu = jnp.mean(x, axis=-1, keepdims=True)
            var = jnp.mean((x - mu) ** 2, axis=-1, keepdims=True)
            return (x - mu) * jax.lax.rsqrt(var + EPS) * g + b
        key = jax.random.key(seed)
        ks = jax.random.split(key, 16)
        s = 0.02
        return {'x': jax.random.normal(ks[0], (B, N, C), jnp.float32), 'ln1_g': jnp.ones((C,), jnp.float32), 'ln1_b': jnp.zeros((C,), jnp.float32), 'Wx': jax.random.normal(ks[1], (C, INNER), jnp.float32) * s, 'bx': jnp.zeros((INNER,), jnp.float32), 'Wq': jax.random.normal(ks[2], (DH, KR), jnp.float32) * s, 'Wk': jax.random.normal(ks[3], (DH, KR), jnp.float32) * s, 'Wv': jax.random.normal(ks[4], (DH, DH), jnp.float32) * s, 'Wo': jax.random.normal(ks[5], (INNER, C), jnp.float32) * s, 'bo': jnp.zeros((C,), jnp.float32), 'ln2_g': jnp.ones((C,), jnp.float32), 'ln2_b': jnp.zeros((C,), jnp.float32), 'W1': jax.random.normal(ks[6], (C, FF), jnp.float32) * s, 'b1': jnp.zeros((FF,), jnp.float32), 'W2': jax.random.normal(ks[7], (FF, C), jnp.float32) * s, 'b2': jnp.zeros((C,), jnp.float32)}
    _L0_mix_all = _L0_mix_setup()
    _L0_mix_in = {k: v for k, v in _L0_mix_all.items() if k in ('ln1_g', 'ln1_b', 'Wx', 'bx', 'Wq', 'Wk', 'Wv', 'Wo', 'bo', 'ln2_g', 'ln2_b', 'W1', 'b1', 'W2', 'b2')}
    del _L0_mix_all

    def _L0_ffn_setup():
        import jax, jax.numpy as jnp
        import numpy as np
        TOP_K = 2
        key = jax.random.key(seed)
        ks = jax.random.split(key, 4)
        B, L, D, H, E = (8, 512, 256, 1024, 8)
        s = 0.02
        return {'x': jax.random.normal(ks[0], (B, L, D), jnp.float32), 'Wg': jax.random.normal(ks[1], (D, E), jnp.float32) * s, 'bg': jnp.zeros((E,), jnp.float32), 'W1': jax.random.normal(ks[2], (E, D, H), jnp.float32) * s, 'b1': jnp.zeros((E, H), jnp.float32), 'W2': jax.random.normal(ks[3], (E, H, D), jnp.float32) * s, 'b2': jnp.zeros((E, D), jnp.float32)}
    _L0_ffn_all = _L0_ffn_setup()
    _L0_ffn_in = {k: v for k, v in _L0_ffn_all.items() if k in ('Wg', 'bg', 'W1', 'b1', 'W2', 'b2')}
    del _L0_ffn_all
    return {'x': x, 'src': src, 'dst': dst, 'L0_gnn_W': _L0_gnn_in['W'], 'L0_gnn_b': _L0_gnn_in['b'], 'L0_mix_ln1_g': _L0_mix_in['ln1_g'], 'L0_mix_ln1_b': _L0_mix_in['ln1_b'], 'L0_mix_Wx': _L0_mix_in['Wx'], 'L0_mix_bx': _L0_mix_in['bx'], 'L0_mix_Wq': _L0_mix_in['Wq'], 'L0_mix_Wk': _L0_mix_in['Wk'], 'L0_mix_Wv': _L0_mix_in['Wv'], 'L0_mix_Wo': _L0_mix_in['Wo'], 'L0_mix_bo': _L0_mix_in['bo'], 'L0_mix_ln2_g': _L0_mix_in['ln2_g'], 'L0_mix_ln2_b': _L0_mix_in['ln2_b'], 'L0_mix_W1': _L0_mix_in['W1'], 'L0_mix_b1': _L0_mix_in['b1'], 'L0_mix_W2': _L0_mix_in['W2'], 'L0_mix_b2': _L0_mix_in['b2'], 'L0_ffn_Wg': _L0_ffn_in['Wg'], 'L0_ffn_bg': _L0_ffn_in['bg'], 'L0_ffn_W1': _L0_ffn_in['W1'], 'L0_ffn_b1': _L0_ffn_in['b1'], 'L0_ffn_W2': _L0_ffn_in['W2'], 'L0_ffn_b2': _L0_ffn_in['b2']}

def reference(x, src, dst, L0_gnn_W, L0_gnn_b, L0_mix_ln1_g, L0_mix_ln1_b, L0_mix_Wx, L0_mix_bx, L0_mix_Wq, L0_mix_Wk, L0_mix_Wv, L0_mix_Wo, L0_mix_bo, L0_mix_ln2_g, L0_mix_ln2_b, L0_mix_W1, L0_mix_b1, L0_mix_W2, L0_mix_b2, L0_ffn_Wg, L0_ffn_bg, L0_ffn_W1, L0_ffn_b1, L0_ffn_W2, L0_ffn_b2):
    import jax
    import jax.numpy as jnp

    def _L0_gnn_ref(x, W, b, edge_src, edge_dst):
        import jax, jax.numpy as jnp
        import numpy as np
        N_NODES = 6250
        N_EDGES = 100000
        IN_SIZE = 256
        OUT_SIZE = 256
        Wh = x @ W + b
        m = Wh[edge_src]
        summed = jax.ops.segment_sum(m, edge_dst, num_segments=N_NODES)
        deg = jax.ops.segment_sum(jnp.ones((edge_dst.shape[0],), dtype=x.dtype), edge_dst, num_segments=N_NODES)
        h = summed / jnp.maximum(deg, 1.0)[:, None]
        return h

    def _L0_mix_ref(x, ln1_g, ln1_b, Wx, bx, Wq, Wk, Wv, Wo, bo, ln2_g, ln2_b, W1, b1, W2, b2):
        import jax, jax.numpy as jnp
        import numpy as np
        B, N, C = (8, 1024, 256)
        HEADS, DH, KR = (8, 32, 4)
        INNER = HEADS * DH
        FF = 4 * C
        EPS = 1e-05

        def layernorm(x, g, b):
            mu = jnp.mean(x, axis=-1, keepdims=True)
            var = jnp.mean((x - mu) ** 2, axis=-1, keepdims=True)
            return (x - mu) * jax.lax.rsqrt(var + EPS) * g + b
        b, n, c = x.shape
        h = layernorm(x, ln1_g, ln1_b)
        xm = h @ Wx + bx
        xm = xm.reshape(b, n, HEADS, DH).transpose(0, 2, 1, 3)
        q = jax.nn.softmax(xm @ Wq, axis=-1)
        k = jax.nn.softmax(xm @ Wk, axis=-2)
        v = xm @ Wv
        kv = jnp.einsum('bhnr,bhnd->bhrd', k, v)
        qkv = jnp.einsum('bhnr,bhrd->bhnd', q, kv)
        attn = qkv.transpose(0, 2, 1, 3).reshape(b, n, INNER) @ Wo + bo
        fx = attn + x
        h2 = layernorm(fx, ln2_g, ln2_b)
        m = jax.nn.gelu(h2 @ W1 + b1, approximate=False) @ W2 + b2
        return m + fx

    def _L0_ffn_ref(x, Wg, bg, W1, b1, W2, b2):
        import jax, jax.numpy as jnp
        import numpy as np
        TOP_K = 2
        B, L, D = x.shape
        E = W1.shape[0]
        xf = x.reshape(-1, D)
        gate_logits = xf @ Wg + bg
        top_w, top_i = jax.lax.top_k(gate_logits, TOP_K)
        top_w = jax.nn.softmax(top_w, axis=-1)
        w_dense = jnp.sum(jax.nn.one_hot(top_i, E, dtype=xf.dtype) * top_w[..., None], axis=1)
        out = jnp.zeros_like(xf)
        for e in range(E):
            h = jax.nn.gelu(xf @ W1[e] + b1[e], approximate=False)
            out = out + w_dense[:, e:e + 1] * (h @ W2[e] + b2[e])
        return out.reshape(B, L, D)
    xn = _layernorm(x, axis=-1)
    x = x + _L0_gnn_ref(xn, L0_gnn_W, L0_gnn_b, src, dst) + _L0_mix_ref(xn[None], L0_mix_ln1_g, L0_mix_ln1_b, L0_mix_Wx, L0_mix_bx, L0_mix_Wq, L0_mix_Wk, L0_mix_Wv, L0_mix_Wo, L0_mix_bo, L0_mix_ln2_g, L0_mix_ln2_b, L0_mix_W1, L0_mix_b1, L0_mix_W2, L0_mix_b2)[0]
    x = x + _L0_ffn_ref(_layernorm(x, axis=-1)[None], L0_ffn_Wg, L0_ffn_bg, L0_ffn_W1, L0_ffn_b1, L0_ffn_W2, L0_ffn_b2)[0]
    return x

_drawn_inputs = setup_inputs


def setup_inputs(seed=0):
    import zlib

    import numpy as np

    out = dict(_drawn_inputs(seed))
    spreads = {'L0_mix_ln1_g': (1.0, 0.6),
     'L0_mix_ln1_b': (0.0, 0.8),
     'L0_mix_bx': (0.0, 0.8),
     'L0_mix_bo': (0.0, 0.579),
     'L0_mix_ln2_g': (1.0, 0.6),
     'L0_mix_ln2_b': (0.0, 2.0),
     'L0_mix_b1': (0.0, 1.39),
     'L0_mix_b2': (0.0, 0.561),
     'L0_ffn_bg': (0.0, 0.889),
     'L0_ffn_b1': (0.0, 1.958),
     'L0_ffn_b2': (0.0, 0.762)}
    factors = {'L0_gnn_b': 10.417,
     'L0_mix_Wx': 8.0,
     'L0_mix_Wq': 8.0,
     'L0_mix_Wk': 8.0,
     'L0_mix_Wv': 8.0,
     'L0_mix_Wo': 8.0,
     'L0_gnn_W': 3.796,
     'L0_ffn_Wg': 2.86,
     'L0_ffn_W1': 4.478}
    for name, (base, spread) in spreads.items():
        noise = np.random.default_rng([zlib.crc32(name.encode()), seed]).standard_normal(out[name].shape)
        drawn = base * np.exp(spread * noise) if base else spread * noise
        out[name] = jnp.asarray(drawn.astype(out[name].dtype))
    for name, factor in factors.items():
        out[name] = (out[name] * factor).astype(out[name].dtype)
    return out
```

```python
from contextlib import ExitStack

import numpy as np

import concourse.bass as bass
from concourse import mybir

F32 = mybir.dt.float32
I32 = mybir.dt.int32
U32 = mybir.dt.uint32
BF16 = mybir.dt.bfloat16
ALU = mybir.AluOpType
ACT = mybir.ActivationFunctionType
X = mybir.AxisListType.X

P = 128
K = 4
R = 8
BATCH = 7
TM = 256
EPS = 1e-5
NO_NODE = 1 << 20
APART = 1 << 21
RSQRT_SEED = 0x5F3759DF


def tiles_of(n_nodes):
    tiles = -(-n_nodes // P)
    return -(-tiles // BATCH) * BATCH


def groups_of(n_edges):
    groups = -(-n_edges // (P * K))
    return -(-groups // R) * R


def row(t, i):
    return t[:, bass.ds(i, 1), :].rearrange("p o c -> p (o c)")


def col(t, i):
    return t[:, bass.ds(i, 1)]


def slot_free(b, i):
    return b * BATCH + (i + 1 if i or BATCH % 2 == 0 else 2)


class Steps:

    def __init__(self, engine, semaphore):
        self.engine, self.semaphore, self.n = engine, semaphore, 0

    def __call__(self, instruction):
        self.n += 1
        instruction.then_inc(self.semaphore, 1)
        self.engine.wait_ge(self.semaphore, self.n)

    def restart(self):
        self.engine.sem_clear(self.semaphore)
        self.n = 0


def build(nc, n_nodes, x, edges, dst_line, dst_next, gnn_W, gnn_b, ln1_g, ln1_b, Wx, bx, Wq, Wk, Wv, Wo, bo,
          ln2_g, ln2_b, W1, b1, W2, b2, Wg, bg, EW1, Eb1, EW2, Eb2, out):
    T = x.shape[0] // P
    NP = T * P
    C = x.shape[1]
    CC = C // P
    NG = edges.shape[0]
    F = W1.shape[1]
    FC = F // P
    DH, KR = Wq.shape
    H = C // DH
    QK = H * KR
    NX = EW1.shape[0]
    CAP = NP + TM
    MT = (2 * NP + NX * (TM - 1)) // TM
    MT += MT % 2
    HALVES = TM // P
    NI = -(-NP // TM)
    GP = NG // R
    NB = T // BATCH
    LAST = n_nodes - (T - 1) * P
    PAD_TILES = [t for t in range(T) if n_nodes - t * P < P]

    table = nc.dram_tensor("xn_table", [NP, C], F32, kind="Internal").ap()
    regions = nc.dram_tensor("expert_rows", [NX * CAP + TM, C + 1], F32, kind="Internal").ap()
    answers = nc.dram_tensor("expert_answers", [2 * NP, C], F32, kind="Internal").ap()

    ctx = ExitStack()
    with ctx:
        def sb(name, shape, dt=F32, scope=ctx):
            return scope.enter_context(nc.sbuf_tensor(name, shape, dt))

        def sem(name):
            return ctx.enter_context(nc.semaphore(name))

        acc = sb("acc", [P, T, C])
        xn = sb("xn", [P, T, C])
        wgt = sb("wgt", [P, 2, T])
        gap = sb("gap", [P, T])
        ident = sb("ident", [P, P])
        ones_b = sb("ones_b", [P, P], BF16)
        eb1 = sb("eb1", [P, NX * FC])
        route_i = sb("route_i", [P, 2 * MT + NX], I32)

        late = ExitStack()
        ew1 = sb("ew1", [P, 2, CC, F], scope=late)
        ew2 = sb("ew2", [P, 2, FC, C], scope=late)
        eb1_t = sb("eb1_t", [P, 2, FC], scope=late)
        eb2_t = sb("eb2_t", [P, 2, C], scope=late)
        xrow = sb("xrow", [P, 2, HALVES, C + 1], scope=late)
        xcol = sb("xcol", [P, CC, TM], scope=late)
        hid = sb("hid", [P, FC, TM], scope=late)
        ans = sb("ans", [P, 2, HALVES, C], scope=late)
        home = sb("home", [P, 2, HALVES], I32, scope=late)
        back = sb("back", [P, 2, 2, BATCH, C], scope=late)
        late.close()

        early = ExitStack()
        scan = ExitStack()
        dline = sb("dline", [P, NG * K], I32, scope=scan)
        dnext = sb("dnext", [P, NG * K], I32, scope=scan)
        below = sb("below", [R, T, GP], scope=scan)
        nbelow = sb("nbelow", [R, T], scope=scan)
        first_i = sb("first_i", [R, GP], I32, scope=scan)
        first = sb("first", [R, GP], scope=scan)
        scan.close()
        G = sb("G", [P, R, K, C + 1], scope=early)
        edge = sb("edge", [P, R, 2 * K], I32, scope=early)
        logit = sb("logit", [P, T, 2 * QK], scope=early)
        gw = sb("gw", [P, CC, C], scope=early)
        w1 = sb("w1", [P, CC, F], scope=early)
        w2 = sb("w2", [P, FC, C], scope=early)
        b1f = sb("b1f", [P, FC], scope=early)
        b2r = sb("b2r", [P, C], scope=early)
        gbr = sb("gbr", [P, C], scope=early)
        wg = sb("wg", [P, CC, NX], scope=early)
        bgr = sb("bgr", [P, NX], scope=early)
        attend = sb("attend", [QK + 1, C], scope=early)
        nw = sb("nw", [P, 2, T], scope=early)
        qT = sb("qT", [QK + 1, P], scope=early)
        taken = sb("taken", [P, NX], BF16, scope=early)
        lane = sb("lane", [P, P], scope=early)
        pcol = sb("pcol", [P, 1], scope=early)
        tok = sb("tok", [P, T], scope=early)
        tbase = sb("tbase", [P, 2, T], scope=early)
        before = sb("before", [P, P], BF16, scope=early)
        padneg = sb("padneg", [P, 1], scope=early)
        region8 = sb("region8", [P, NX + 1], scope=early)
        wrong = sb("wrong", [P, 1], scope=early)
        fsum = sb("fsum", [P, 1], scope=early)
        ones_f = sb("ones_f", [P, P], scope=early)
        bounds = sb("bounds", [P, T + 3], I32, scope=early)
        mlane = sb("mlane", [P, MT], scope=early)
        nlane = sb("nlane", [P, NI], scope=early)
        filler = sb("filler", [P, C + 1], scope=early)

        setup = ExitStack()
        wx = sb("wx", [P, CC, C], scope=setup)
        wxT = sb("wxT", [P, CC, C], scope=setup)
        wo = sb("wo", [P, CC, C], scope=setup)
        heads = sb("heads", [P, CC, 2 * QK + C], scope=setup)
        fold = sb("fold", [P, CC, 2 * QK + C], scope=setup)
        foldg = sb("foldg", [P, CC, 2 * QK + C], scope=setup)
        fconst = sb("fconst", [P, 2 * QK + C], scope=setup)
        rep = sb("rep", [P, 2, CC, P], scope=setup)
        lncol = sb("lncol", [P, 5, CC], scope=setup)
        z = sb("z", [P, 2, C + 1], scope=setup)
        zT = sb("zT", [P, 2, CC, P], scope=setup)
        ek = sb("ek", [P, 2, QK], scope=setup)
        kmax = sb("kmax", [P, QK], scope=setup)
        kcol = sb("kcol", [QK, 1], scope=setup)
        kspread = sb("kspread", [QK, P], scope=setup)
        kz = sb("kz", [QK, C + 2], scope=setup)
        kzT = sb("kzT", [P, CC, QK], scope=setup)
        kv = sb("kv", [QK, C], scope=setup)
        kvT = sb("kvT", [P, CC, QK], scope=setup)
        hmask = sb("hmask", [QK, C], scope=setup)
        head_of = sb("head_of", [QK, 1], scope=setup)
        hmask_i = sb("hmask_i", [QK, C], I32, scope=setup)
        zero = sb("zero", [P, P], BF16, scope=setup)
        zrow = sb("zrow", [P, C + 1], BF16, scope=setup)
        iot = sb("iot", [P, P], I32, scope=setup)
        tok_i = sb("tok_i", [P, T], I32, scope=setup)
        mlane_i = sb("mlane_i", [P, MT], I32, scope=setup)
        pcol_i = sb("pcol_i", [P, 2], I32, scope=setup)
        stats7 = sb("stats7", [P, BATCH, 6], scope=setup)
        mvb = sb("mvb", [P, BATCH, 2], scope=setup)
        rsb = sb("rsb", [P, BATCH], scope=setup)
        mv = sb("mv", [P, T, 2], scope=setup)
        rs = sb("rs", [P, T], scope=setup)
        qred = sb("qred", [P, T * H], scope=setup)
        b1c = sb("b1c", [P, FC], scope=setup)
        tend = sb("tend", [P, T], scope=setup)
        gl = sb("gl", [P, 3, T], scope=setup)
        setup.close()
        tiles = ExitStack()
        onehot = sb("onehot", [P, K, P], scope=tiles)
        q_t = sb("q_t", [P, QK], scope=tiles)
        fx = sb("fx", [P, C], scope=tiles)
        z2 = sb("z2", [P, C], scope=tiles)
        z2T = sb("z2T", [P, CC, P], scope=tiles)
        hT = sb("hT", [P, FC, P], scope=tiles)
        agg = sb("agg", [P, C], scope=tiles)
        aggT = sb("aggT", [P, CC, P], scope=tiles)
        part = sb("part", [P, C], scope=tiles)
        deg = sb("deg", [P, 3], scope=tiles)
        node = sb("node", [P, 2, P], scope=tiles)
        sent = sb("sent", [P, 2, C + 1], scope=tiles)
        z3T = sb("z3T", [P, CC, P], scope=tiles)
        lg = sb("lg", [P, NX], scope=tiles)
        top = sb("top", [P, 8], scope=tiles)
        top_i = sb("top_i", [P, 8], U32, scope=tiles)
        choice = sb("choice", [P, 2], scope=tiles)
        pick = sb("pick", [P, 2, NX], scope=tiles)
        both = sb("both", [P, NX], BF16, scope=tiles)
        slot = sb("slot", [P, NX], scope=tiles)
        slots = sb("slots", [P, 2, NX], scope=tiles)
        place = sb("place", [P, 2], scope=tiles)
        place_i = sb("place_i", [P, 2], I32, scope=tiles)
        stats = sb("stats", [P, 6], scope=tiles)
        mv1 = sb("mv1", [P, 2], scope=tiles)
        rs1 = sb("rs1", [P, 1], scope=tiles)
        cnt = sb("cnt", [P, 4, NX], scope=tiles)
        many = sb("many", [P, NX, NI], scope=tiles)
        base9 = sb("base9", [P, NX + 1], scope=tiles)
        done = sb("done", [P, MT, NX + 1], scope=tiles)
        mrow = sb("mrow", [P, 3, MT], scope=tiles)
        tiles.close()
        early.close()

        bank = [ctx.enter_context(nc.psum_tensor(f"bank{i}", [P, 512], F32)) for i in range(8)]

        names = """weights_loaded blocks_loaded edges_scanned heads_zeroed pool_ready
            steps_dve xn_done table_stored columns_repeated bounds_counted bounds_done wx_transposed
            wxT_copied folded fold_copied constants_folded
            z_done z_transposed zT_copied logits_done logits_taken
            kmax_done kmax_transposed kmax_spread kmax_back logits_ready q_exp ek_done kz_done
            kz_scaled kz_transposed kzT_copied kv_done kv_masked kv_transposed kvT_copied
            attend_done attend_copied
            ring_has_ones groups_free groups_ready onehot_done onehot_used
            q_staged q_transposed qT_copied fx_done z2_done z2_transposed z2T_copied
            hidden_a hidden_b gelu_a gelu_b agg_done agg_transposed aggT_copied
            z3_done z3_transposed z3T_copied gates_done picks_done ranks_done places_done scattered
            scatters_begun gathers_begun answers_begun
            y_done taken_done picks_counted tables_done filled
            rows_transposed rows_copied expert_y answer_done weights_done
            out_done out_stored""".split()
        S = {n: sem(n) for n in names}
        x_in = [sem(f"x_in{b}") for b in range(NB)]
        edge_in = [sem(f"edge_in{r}") for r in range(R)]
        gathered = [sem(f"gathered{r}") for r in range(R)]
        hidden = [sem(f"hidden{i}") for i in range(FC // 2)]
        gelued = [sem(f"gelued{i}") for i in range(FC // 2)]
        expert_in = [sem(f"expert_in{j}") for j in range(2)]
        expert_out = [sem(f"expert_out{j}") for j in range(2)]
        back_in = [sem(f"back_in{b}") for b in range(2)]

        N_WEIGHTS = 17
        block = ctx.enter_context(nc.Block())

        @block.sync
        def _(sp):
            for b in range(NB):
                sp.dma_start(acc[:, b * BATCH:(b + 1) * BATCH, :],
                             x[b * BATCH * P:(b + 1) * BATCH * P, :].rearrange("(t p) c -> p t c", p=P)
                             ).then_inc(x_in[b], 16)
            sp.dma_start(dline[:], dst_line.rearrange("(p n) -> p n", p=P)).then_inc(S["edges_scanned"], 16)
            sp.dma_start(dnext[:], dst_next.rearrange("(p n) -> p n", p=P)).then_inc(S["edges_scanned"], 16)
            sp.dma_start(first_i[:], edges[:, 0:1, K:K + 1].rearrange("(r g) a b -> r (g a b)", r=R),
                         allow_slow_non_contiguous=True).then_inc(S["edges_scanned"], 16)
            for tile, src in ((wx, Wx), (wo, Wo), (gw, gnn_W), (w1, W1), (w2, W2), (wg, Wg)):
                sp.dma_start(tile[:], src.rearrange("(c p) n -> p c n", p=P)).then_inc(S["weights_loaded"], 16)
            for n, src in enumerate((ln1_g, ln1_b, ln2_g, ln2_b, bx)):
                sp.dma_start(lncol[:, n, :], src.rearrange("(c p) -> p c", p=P),
                             allow_slow_non_contiguous=True).then_inc(S["weights_loaded"], 16)
            sp.dma_start(b1c[:], b1.rearrange("(c p) -> p c", p=P), allow_slow_non_contiguous=True).then_inc(S["weights_loaded"], 16)
            sp.dma_start(b2r[:], b2.partition_broadcast(P)).then_inc(S["weights_loaded"], 16)
            sp.dma_start(gbr[:], gnn_b.partition_broadcast(P)).then_inc(S["weights_loaded"], 16)
            sp.dma_start(bgr[:], bg.partition_broadcast(P)).then_inc(S["weights_loaded"], 16)
            sp.dma_start(attend[QK:QK + 1, :], bo.partition_broadcast(1)).then_inc(S["weights_loaded"], 16)
            sp.dma_start(eb1[:].rearrange("p (e c) -> p e c", e=NX), Eb1.rearrange("e (c p) -> p e c", p=P),
                         allow_slow_non_contiguous=True).then_inc(S["weights_loaded"], 16)
            sp.wait_ge(S["heads_zeroed"], 1)
            for h in range(H):
                at, cc = h * DH % P, h * DH // P
                for start, width, src in ((KR * h, KR, Wq), (QK + KR * h, KR, Wk), (2 * QK + DH * h, DH, Wv)):
                    sp.dma_start(heads[at:at + DH, cc, start:start + width], src).then_inc(S["blocks_loaded"], 16)
            for b in range(NB):
                sp.wait_ge(S["xn_done"], BATCH * (b + 1))
                sp.dma_start(table[b * BATCH * P:(b + 1) * BATCH * P, :].rearrange("(t p) c -> p t c", p=P),
                             xn[:, b * BATCH:(b + 1) * BATCH, :]).then_inc(S["table_stored"], 16)
            sp.wait_ge(S["bounds_done"], 1)
            laps = sp.value_load(bounds[0:1, T + 2:T + 3], min_val=1, max_val=T)
            with sp.Fori(0, laps) as lap:
                with sp.Fori(0, NG // R) as b:
                    for r in range(R):
                        sp.wait_ge(S["groups_free"], lap * NG + b * R + (r + 1))
                        sp.dma_start(edge[:, r, :], edges[bass.ds(b * R + r, 1), :, :]
                                     .rearrange("o p k -> (o p) k")).then_inc(edge_in[r], 16)

            def load_expert(i, j):
                expert = sp.value_load(route_i[0:1, bass.ds(i, 1)], min_val=0, max_val=NX - 1)
                start = sp.value_load(route_i[0:1, bass.ds(i + MT, 1)], min_val=0, max_val=NX * CAP)
                sp.dma_start(xrow[:, j, :, :], regions[bass.ds(start, TM), :]
                             .rearrange("(h p) c -> p h c", p=P)).then_inc(expert_in[j], 16)
                sp.dma_start(ew1[:, j, :, :], EW1[bass.ds(expert, 1), :, :]
                             .rearrange("o (c p) f -> p (o c) f", p=P)).then_inc(expert_in[j], 16)
                sp.dma_start(ew2[:, j, :, :], EW2[bass.ds(expert, 1), :, :]
                             .rearrange("o (c p) f -> p (o c) f", p=P)).then_inc(expert_in[j], 16)
                sp.dma_start(eb1_t[:, j, :], eb1[:, bass.ds(expert * FC, FC)]).then_inc(expert_in[j], 16)
                sp.dma_start(eb2_t[:, j, :], Eb2[bass.ds(expert, 1), :].rearrange("o c -> (o c)")
                             .partition_broadcast(P)).then_inc(expert_in[j], 16)

            sp.wait_ge(S["tables_done"], 1)
            for e in range(NX):
                start = sp.value_load(route_i[0:1, 2 * MT + e:2 * MT + e + 1], min_val=0, max_val=NX * CAP)
                for h in range(HALVES):
                    sp.dma_start(regions[bass.ds(start + h * P, P), :], filler[:]).then_inc(S["filled"], 16)
            for h in range(HALVES):
                sp.dma_start(regions[NX * CAP + h * P:NX * CAP + (h + 1) * P, :], filler[:]).then_inc(S["filled"], 16)
            sp.wait_ge(S["filled"], 16 * HALVES * (NX + 1))
            sp.wait_ge(S["scattered"], 32 * T)
            for j in range(2):
                load_expert(j, j)
            with sp.Fori(1, MT // 2) as pair:
                for j in range(2):
                    sp.wait_ge(S["answer_done"], pair * 2 + j)
                    load_expert(pair * 2 + j, j)

            for j in range(2):
                sp.wait_ge(expert_out[j], 16 * HALVES * (MT // 2))
            for b in range(NB):
                if b >= 2:
                    sp.wait_ge(S["out_done"], 2 * BATCH * (b - 1))
                for k in range(2):
                    at = k * NP + b * BATCH * P
                    sp.dma_start(back[:, b % 2, k, :, :], answers[at:at + BATCH * P, :]
                                 .rearrange("(t p) c -> p t c", p=P)).then_inc(back_in[b % 2], 16)

        @block.gpsimd
        def _(pool):
            nc.gpsimd.iota(iot[:], pattern=[[1, P]], base=0, channel_multiplier=0)
            nc.gpsimd.iota(pcol_i[:, 0:1], pattern=[[0, 1]], base=0, channel_multiplier=1)
            nc.gpsimd.iota(tok_i[:], pattern=[[P, T]], base=0, channel_multiplier=1)
            nc.gpsimd.iota(mlane_i[:], pattern=[[1, MT]], base=0, channel_multiplier=0)
            nc.gpsimd.iota(hmask_i[:], pattern=[[1, H], [0, DH]], base=0, channel_multiplier=0)
            nc.gpsimd.memset(heads[:], 0.0).then_inc(S["heads_zeroed"], 1)
            nc.gpsimd.memset(taken[:], 0.0)
            nc.gpsimd.memset(zero[:], 0.0)
            nc.gpsimd.memset(zrow[:], 0.0)
            nc.gpsimd.memset(ones_b[:], 1.0)
            nc.gpsimd.memset(ones_f[:], 1.0)
            nc.gpsimd.memset(z[:, :, C:C + 1], 1.0)
            nc.gpsimd.memset(filler[:, 0:C], 0.0)
            nc.gpsimd.memset(filler[:, C:C + 1], float(2 * NP)).then_inc(S["pool_ready"], 1)

            def scatter(s):
                pool.wait_ge(S["places_done"], s + 1)
                pool.sem_inc(S["scatters_begun"], 1)
                for k in range(2):
                    pool.indirect_dma_start(out=regions[:, :],
                                            out_offset=bass.IndirectOffsetOnAxis(ap=place_i[:, k:k + 1], axis=0),
                                            in_=sent[:, k, :], in_offset=None).then_inc(S["scattered"], 16)

            pool.wait_ge(S["bounds_done"], 1)
            nc.gpsimd.memset(G[:, :, :, C:C + 1], 1.0).then_inc(S["ring_has_ones"], 1)
            laps = pool.value_load(bounds[0:1, T + 2:T + 3], min_val=1, max_val=T)
            next_tile = pool.alloc_register("next_tile")
            its_end = pool.alloc_register("its_end")
            pool.reg_mov(next_tile, 0)
            pool.reg_load(its_end, bounds[0:1, 2:3])
            pool.wait_ge(S["table_stored"], 16 * NB)
            def fill_ring(b, blocks, first):
                for r in range(R):
                    pool.wait_ge(edge_in[r], blocks * 16)
                    pool.sem_inc(S["gathers_begun"], 1)
                    for k in range(K):
                        pool.indirect_dma_start(
                            out=G[:, r, k, 0:C], out_offset=None, in_=table[:, :],
                            in_offset=bass.IndirectOffsetOnAxis(ap=edge[:, r, k:k + 1], axis=0)
                        ).then_inc(gathered[r], 16)
                    if r > 0:
                        pool.wait_ge(gathered[r - 1], blocks * (16 * K))
                    elif not first:
                        pool.wait_ge(gathered[R - 1], b * (16 * K))
                    pool.sem_inc(S["groups_ready"], 1)
                with pool.While(lambda: pool.snap(its_end) < blocks * R - 1):
                    scatter(pool.snap(next_tile, min_val=0, max_val=T - 1))
                    pool.reg_add(next_tile, next_tile, 1)
                    pool.reg_load(its_end, bounds[0:1, bass.ds(pool.snap(next_tile, min_val=0, max_val=T - 1) + 2, 1)])

            fill_ring(0, 1, True)
            with pool.Fori(1, laps * (NG // R)) as b:
                fill_ring(b, pool.snap(b + 1), False)
            pool.wait_ge(gathered[R - 1], laps * (NG // R) * (16 * K))
            pool.sem_inc(S["groups_ready"], 1)
            with pool.Fori(pool.snap(next_tile, min_val=0, max_val=T - 1), T) as s:
                scatter(s)

            with pool.Fori(0, MT // 2) as pair:
                for j in range(2):
                    pool.wait_ge(S["answer_done"], pair * 2 + (j + 2))
                    pool.sem_inc(S["answers_begun"], 1)
                    for h in range(HALVES):
                        pool.indirect_dma_start(out=answers[:, :],
                                                out_offset=bass.IndirectOffsetOnAxis(ap=home[:, j, h:h + 1], axis=0),
                                                in_=ans[:, j, h, :], in_offset=None,
                                                bounds_check=2 * NP - 1, oob_is_err=False
                                                ).then_inc(expert_out[j], 16)

        @block.vector
        def _(dve):
            v = nc.vector
            step = Steps(dve, S["steps_dve"])

            def rsqrt(y, var, width):
                ve, t = nw[:, 0, 0:width], nw[:, 1, 0:width]
                step(v.tensor_scalar(ve, var, EPS, None, ALU.add))
                step(v.tensor_scalar(t.bitcast(I32), ve.bitcast(I32), 1, None, ALU.logical_shift_right))
                step(v.tensor_scalar(y.bitcast(I32), t.bitcast(I32), -1.0, float(RSQRT_SEED), ALU.mult, ALU.add))
                for _ in range(3):
                    step(v.tensor_tensor(t, y, y, ALU.mult))
                    step(v.scalar_tensor_tensor(t, t, -0.5, ve, ALU.mult, ALU.mult))
                    step(v.scalar_tensor_tensor(y, t, 1.5, y, ALU.add, ALU.mult))

            def spread(src, tiles):
                for i, t in enumerate(tiles):
                    ins = v.bn_stats(stats7[:, i, :], row(src, t))
                step(ins)
                for i in range(BATCH):
                    ins = v.bn_aggr(mvb[:, i, :], stats7[:, i, :])
                step(ins)
                rsqrt(rsb[:], mvb[:, :, 1], BATCH)

            def bc(ap, shape):
                return ap.to_broadcast(shape)

            for b in range(NB):
                dve.wait_ge(x_in[b], 16)
                spread(acc, [b * BATCH + i for i in range(BATCH)])
                for i in range(BATCH):
                    v.tensor_scalar(xn[:, b * BATCH + i, :], acc[:, b * BATCH + i, :], mvb[:, i, 0:1], rsb[:, i:i + 1],
                                    ALU.subtract, ALU.mult).then_inc(S["xn_done"], 1)

            dve.wait_ge(S["pool_ready"], 1)
            step(v.memset(qT[QK:QK + 1, :], 1.0))
            step(v.tensor_copy(lane[:], iot[:]))
            step(v.tensor_copy(pcol[:], pcol_i[:, 0:1]))
            step(v.tensor_copy(tok[:], tok_i[:]))
            step(v.tensor_copy(mlane[:], mlane_i[:]))
            step(v.tensor_scalar(nlane[:], mlane[:, 0:NI], float(TM), None, ALU.mult))
            step(v.tensor_scalar(ident[:], lane[:], pcol[:], None, ALU.is_equal))
            step(v.tensor_scalar(before[:], lane[:], pcol[:], None, ALU.is_gt))
            step(v.tensor_scalar(padneg[:], pcol[:], float(LAST), -1e30, ALU.is_ge, ALU.mult))
            step(v.tensor_scalar(region8[:], lane[:, 0:NX + 1], float(CAP), None, ALU.mult))
            step(v.tensor_scalar(tbase[:, 0, :], mlane[:, 0:T], float(P), None, ALU.mult))
            step(v.tensor_scalar(tend[:], tbase[:, 0, :], float(P), None, ALU.add))
            step(v.tensor_scalar(pcol_i[0:QK, 1:2], pcol_i[0:QK, 0:1], KR.bit_length() - 1, None,
                                 ALU.logical_shift_right))
            step(v.tensor_copy(head_of[:], pcol_i[0:QK, 1:2]))
            step(v.tensor_copy(hmask[:], hmask_i[:]))
            step(v.tensor_scalar(hmask[:], hmask[:], head_of[:], None, ALU.is_equal))
            dve.wait_ge(S["edges_scanned"], 48)
            step(v.tensor_tensor(dline[:], dline[:], dnext[:], ALU.is_gt))
            step(v.tensor_reduce(wrong[:], dline[:], X, ALU.add))
            step(v.tensor_copy(first[:], first_i[:]))
            step(v.tensor_tensor(below[:], bc(first[:].unsqueeze(1), [R, T, GP]),
                                 bc(tend[0:R, :].unsqueeze(2), [R, T, GP]), ALU.is_lt))
            step(v.tensor_reduce(nbelow[:], below[:], X, ALU.add))
            dve.wait_ge(S["weights_loaded"], 16 * N_WEIGHTS)
            step(v.tensor_copy(rep[:, 0, :, :], bc(lncol[:, 1, :].unsqueeze(2), [P, CC, P])))
            v.tensor_copy(rep[:, 1, :, :], bc(lncol[:, 4, :].unsqueeze(2), [P, CC, P])).then_inc(S["columns_repeated"], 1)
            dve.wait_ge(S["bounds_counted"], 1)
            step(v.tensor_scalar(gl[:, 0, :], bank[0][:, 0:T], -1.0, 0.0, ALU.add, ALU.max))
            step(v.tensor_scalar(gl[:, 0, T - 1:T], gl[:, 0, T - 1:T], float(NG - 1), None, ALU.max))
            step(v.tensor_scalar(fsum[:], bank[1][:, 0:1], 1.0, None, ALU.min))
            step(v.tensor_scalar(gl[:, 1, :], tbase[:, 0, :], float(NG) / P, float(NG - 1), ALU.mult, ALU.add))
            step(v.tensor_tensor(gl[:, 1, :], gl[:, 1, :], gl[:, 0, :], ALU.subtract))
            step(v.scalar_tensor_tensor(gl[:, 0, :], gl[:, 1, :], fsum[:], gl[:, 0, :], ALU.mult, ALU.add))
            step(v.tensor_copy(bounds[:, 1:T + 1], gl[:, 0, :]))
            step(v.memset(bounds[:, 0:1], 0))
            step(v.memset(bounds[:, T + 1:T + 2], 1 << 30))
            step(v.tensor_scalar(wrong[:], fsum[:], float(APART), None, ALU.mult))
            step(v.tensor_scalar(tbase[:, 1, :], tbase[:, 0, :], wrong[:], None, ALU.add))
            step(v.tensor_copy(tbase[:, 1, 0:1], tbase[:, 0, 0:1]))
            v.tensor_scalar(bounds[:, T + 2:T + 3], fsum[:], float(T - 1), 1.0, ALU.mult, ALU.add
                            ).then_inc(S["bounds_done"], 1)
            dve.wait_ge(S["wx_transposed"], 1)
            for i in range(CC):
                ins = v.tensor_copy(wxT[:, i, :], bank[6 + i][:, 0:C])
            ins.then_inc(S["wxT_copied"], 1)
            dve.wait_ge(S["folded"], 1)
            for c in range(CC):
                step(v.tensor_copy(fold[:, c, :], bank[2 + c][:, 0:2 * QK + C]))
            for c in range(CC):
                ins = v.tensor_scalar(foldg[:, c, :], fold[:, c, :], lncol[:, 0, c:c + 1], None, ALU.mult)
            step(ins)
            dve.sem_inc(S["fold_copied"], 1)
            dve.wait_ge(S["constants_folded"], 1)
            for c in range(CC):
                v.tensor_scalar(w1[:, c, :], w1[:, c, :], lncol[:, 2, c:c + 1], None, ALU.mult)
            step(v.tensor_copy(fconst[:], bank[4][:, 0:2 * QK + C]))
            step(v.tensor_tensor(b1f[:], bank[5][:, 0:FC], b1c[:], ALU.add))

            dve.sem_inc(S["logits_taken"], 1)
            with dve.Fori(0, NB) as b:
                step.restart()
                spread(xn, [b * BATCH + i for i in range(BATCH)])
                step(v.tensor_copy(mv[:, bass.ds(b * BATCH, BATCH), :], mvb[:]))
                step(v.tensor_copy(rs[:, bass.ds(b * BATCH, BATCH)], rsb[:]))
                for i in range(BATCH):
                    t = b * BATCH + i
                    dve.wait_ge(S["z_transposed"], slot_free(b, i))
                    v.tensor_scalar(z[:, i % 2, 0:C], row(xn, t), mvb[:, i, 0:1], rsb[:, i:i + 1],
                                    ALU.subtract, ALU.mult).then_inc(S["z_done"], 1)
                dve.wait_ge(S["logits_done"], (b + 1) * BATCH + 2)
                v.tensor_tensor(logit[:, bass.ds(b * BATCH, BATCH), :],
                                bank[6][:, 0:BATCH * 2 * QK].rearrange("p (t c) -> p t c", t=BATCH),
                                bc(fconst[:, 0:2 * QK].unsqueeze(1), [P, BATCH, 2 * QK]),
                                ALU.add).then_inc(S["logits_taken"], 1)
            dve.wait_ge(S["logits_taken"], 1 + NB)
            for t in PAD_TILES:
                if n_nodes > t * P:
                    step(v.tensor_scalar(logit[:, t, QK:], logit[:, t, QK:], padneg[:], None, ALU.add))
                else:
                    step(v.tensor_scalar(logit[:, t, QK:], logit[:, t, QK:], -1e30, None, ALU.add))
            q = logit[:, :, 0:QK].rearrange("p t (h r) -> p t h r", r=KR)
            red = qred[:].rearrange("p (t h) -> p t h", t=T)
            redb = bc(red.unsqueeze(3), [P, T, H, KR])
            k_all = logit[:, :, QK:]
            v.tensor_reduce(kmax[:], k_all.rearrange("p t c -> p c t"), X, ALU.max).then_inc(S["kmax_done"], 1)
            step(v.tensor_reduce(red, q, X, ALU.max))
            dve.wait_ge(S["kmax_transposed"], 1)
            step(v.tensor_reduce(kcol[:], bank[0][0:QK, 0:P], X, ALU.max))
            v.tensor_copy(kspread[:], bc(kcol[:], [QK, P])).then_inc(S["kmax_spread"], 1)
            step(v.tensor_tensor(q, q, redb, ALU.subtract))
            dve.wait_ge(S["kmax_back"], 1)
            step(v.tensor_copy(kmax[:], bank[1][:, 0:QK]))
            v.tensor_tensor(k_all, k_all, bc(kmax[:].unsqueeze(1), [P, T, QK]), ALU.subtract).then_inc(S["logits_ready"], 1)
            dve.wait_ge(S["q_exp"], 1)
            step(v.tensor_reduce(red, q, X, ALU.add))
            step(v.reciprocal(qred[:], qred[:]))
            step(v.tensor_tensor(q, q, redb, ALU.mult))
            with dve.Fori(0, NB) as b:
                for i in range(BATCH):
                    t = b * BATCH + i
                    dve.wait_ge(S["kz_done"], slot_free(b, i))
                    v.tensor_scalar(z[:, i % 2, 0:C], row(xn, t), row(mv, t)[:, 0:1], col(rs, t),
                                    ALU.subtract, ALU.mult).then_inc(S["z_done"], 1)
            dve.wait_ge(S["kz_done"], 2 + T)
            step(v.tensor_copy(kz[:, 0:C + 1], bank[7][0:QK, 0:C + 1]))
            step(v.reciprocal(kz[:, C + 1:C + 2], kz[:, C:C + 1]))
            v.tensor_scalar(kz[:, 0:C], kz[:, 0:C], kz[:, C + 1:C + 2], None, ALU.mult).then_inc(S["kz_scaled"], 1)
            dve.wait_ge(S["kz_transposed"], 1)
            v.tensor_copy(kzT[:].rearrange("p c q -> p (c q)"), bank[0][:, 0:CC * QK]).then_inc(S["kzT_copied"], 1)
            dve.wait_ge(S["kv_done"], 1)
            step(v.tensor_tensor(kv[:], bank[1][0:QK, 0:C], fconst[0:QK, 2 * QK:], ALU.add))
            v.tensor_tensor(kv[:], kv[:], hmask[:], ALU.mult).then_inc(S["kv_masked"], 1)
            dve.wait_ge(S["kv_transposed"], 1)
            v.tensor_copy(kvT[:].rearrange("p c q -> p (c q)"), bank[2][:, 0:CC * QK]).then_inc(S["kvT_copied"], 1)
            dve.wait_ge(S["attend_done"], 1)
            v.tensor_copy(attend[0:QK, :], bank[3][0:QK, 0:C]).then_inc(S["attend_copied"], 1)

            def visit(t, u, nodes):
                dve.wait_ge(S["groups_ready"], u + 2)
                for pair in range(K // 2):
                    dve.wait_ge(S["onehot_used"], (u + t) * 2 + (pair + 1))
                    for k in (2 * pair, 2 * pair + 1):
                        ins = v.tensor_scalar(onehot[:, k, :], nodes, row(edge, u % R)[:, K + k:K + k + 1], None,
                                              ALU.is_equal)
                    ins.then_inc(S["onehot_done"], 1)

            def attention(t, tp1):
                v.tensor_copy(q_t[:], row(logit, t)[:, 0:QK]).then_inc(S["q_staged"], 1)
                step(v.tensor_scalar(node[:, 0, :], lane[:], tbase[:, 0, :][:, bass.ds(t, 1)], None, ALU.add))
                step(v.tensor_scalar(node[:, 1, :], lane[:], tbase[:, 1, :][:, bass.ds(t, 1)], None, ALU.add))
                dve.wait_ge(S["fx_done"], tp1)
                step(v.tensor_tensor(fx[:], bank[2][:, 0:C], row(xn, t), ALU.add))
                step(v.bn_stats(stats[:], fx[:]))
                step(v.bn_aggr(mv1[:], stats[:]))
                rsqrt(rs1[:], mv1[:, 1:2], 1)
                v.tensor_scalar(z2[:], fx[:], mv1[:, 0:1], rs1[:], ALU.subtract, ALU.mult).then_inc(S["z2_done"], 1)
                step(v.tensor_tensor(part[:], row(acc, t), fx[:], ALU.add))
                step(v.tensor_tensor(part[:], part[:], b2r[:], ALU.add))

            def edges_of(t):
                lo = dve.value_load(bounds[0:1, bass.ds(t, 1)], min_val=0, max_val=T * NG)
                hi = dve.value_load(bounds[0:1, bass.ds(t + 1, 1)], min_val=0, max_val=T * NG)
                visit(t, lo, node[:, 1, :])
                with dve.If(lo < hi):
                    with dve.Fori(lo + 1, hi + 1) as u:
                        visit(t, u, node[:, 0, :])
                dve.wait_ge(S["onehot_used"], (hi + t) * 2 + 4)

            def mean(t):
                sums = bank[0]
                step(v.tensor_scalar(deg[:, 0:1], sums[:, C:C + 1], 1.0, None, ALU.max))
                step(v.reciprocal(deg[:, 1:2], deg[:, 0:1]))
                v.tensor_scalar(agg[:], sums[:, 0:C], deg[:, 1:2], None, ALU.mult).then_inc(S["agg_done"], 1)
                step(v.tensor_tensor(deg[:, 2:3], sums[:, C:C + 1], deg[:, 1:2], ALU.mult))
                step(v.scalar_tensor_tensor(part[:], gbr[:], deg[:, 2:3], part[:], ALU.mult, ALU.add))

            def route(s, sp1):
                step(v.bn_stats(stats[:], row(acc, s)))
                step(v.bn_aggr(mv1[:], stats[:]))
                rsqrt(rs1[:], mv1[:, 1:2], 1)
                v.tensor_scalar(sent[:, 0, 0:C], row(acc, s), mv1[:, 0:1], rs1[:], ALU.subtract,
                                ALU.mult).then_inc(S["z3_done"], 1)
                step(v.tensor_scalar(sent[:, 1, 0:C], row(acc, s), mv1[:, 0:1], rs1[:], ALU.subtract, ALU.mult))
                step(v.tensor_scalar(sent[:, 0, C:C + 1], col(tok, s), 0.0, None, ALU.add))
                step(v.tensor_scalar(sent[:, 1, C:C + 1], col(tok, s), float(NP), None, ALU.add))
                dve.wait_ge(S["gates_done"], sp1)
                step(v.tensor_tensor(lg[:], bank[3][:, C:C + NX], bgr[:], ALU.add))
                step(v.max(top[:], lg[:]))
                step(v.max_index(top_i[:], top[:], lg[:]))
                step(v.tensor_copy(choice[:], top_i[:, 0:2]))
                for k in range(2):
                    step(v.tensor_scalar(pick[:, k, :], lane[:, 0:NX], choice[:, k:k + 1], None, ALU.is_equal))
                v.tensor_tensor(both[:], pick[:, 0, :], pick[:, 1, :], ALU.add).then_inc(S["picks_done"], 1)
                step(v.tensor_tensor(col(gap, s), top[:, 1:2], top[:, 0:1], ALU.subtract))
                dve.wait_ge(S["ranks_done"], sp1)
                step(v.tensor_tensor(slot[:], bank[3][:, C + NX:C + 2 * NX], region8[:, 0:NX], ALU.add))
                step(v.tensor_tensor(taken[:], taken[:], both[:], ALU.add))
                step(v.tensor_tensor(slots[:], pick[:], bc(slot[:].unsqueeze(1), [P, 2, NX]), ALU.mult))
                step(v.tensor_reduce(place[:], slots[:], X, ALU.add))
                v.tensor_copy(place_i[:], place[:]).then_inc(S["places_done"], 1)

            def finish(t, tp1):
                dve.wait_ge(S["y_done"], tp1)
                step(v.tensor_tensor(row(acc, t), bank[4][:, 0:C], part[:], ALU.add))

            def tile(t, tp1, earlier):
                step.restart()
                attention(t, tp1)
                edges_of(t)
                mean(t)
                if earlier != "none":
                    if earlier == "some":
                        dve.wait_ge(S["scattered"], (t - 1) * 32)
                    route(dve.snap(t - 1) if earlier == "some" else 0, t)
                finish(t, tp1)

            dve.wait_ge(S["attend_copied"], 1)
            tile(0, 1, "none")
            tile(1, 2, "first")
            with dve.Fori(2, T) as t:
                tile(t, dve.snap(t + 1), "some")
            step.restart()
            dve.wait_ge(S["scattered"], (T - 1) * 32)
            route(T - 1, T)

            dve.wait_ge(S["picks_counted"], 1)
            count, n_tiles, ends, starts = (cnt[:, i, :] for i in range(4))
            step(v.tensor_copy(count, bank[0][:, 0:NX]))
            step(v.tensor_tensor(many[:], bc(count.unsqueeze(2), [P, NX, NI]), bc(nlane[:].unsqueeze(1), [P, NX, NI]),
                                 ALU.is_gt))
            step(v.tensor_reduce(n_tiles, many[:], X, ALU.add))
            step(v.tensor_tensor_scan(ends, ones_f[:, 0:NX], n_tiles, 0.0, ALU.mult, ALU.add))
            step(v.tensor_tensor(starts, ends, n_tiles, ALU.subtract))
            step(v.tensor_copy(base9[:], region8[:]))
            step(v.scalar_tensor_tensor(base9[:, 0:NX], starts, -float(TM), region8[:, 0:NX], ALU.mult, ALU.add))
            step(v.tensor_tensor(done[:, :, 0:NX], bc(ends.unsqueeze(1), [P, MT, NX]),
                                 bc(mlane[:].unsqueeze(2), [P, MT, NX]), ALU.is_le))
            expert, alive, start = (mrow[:, i, :] for i in range(3))
            step(v.tensor_reduce(expert, done[:, :, 0:NX], X, ALU.add))
            step(v.tensor_tensor(done[:], bc(lane[:, 0:NX + 1].unsqueeze(1), [P, MT, NX + 1]),
                                 bc(expert.unsqueeze(2), [P, MT, NX + 1]), ALU.is_equal))
            step(v.tensor_tensor(done[:], done[:], bc(base9[:].unsqueeze(1), [P, MT, NX + 1]), ALU.mult))
            step(v.tensor_reduce(start, done[:], X, ALU.add))
            step(v.tensor_scalar(alive, expert, float(NX), float(TM), ALU.is_lt, ALU.mult))
            step(v.tensor_tensor(alive, alive, mlane[:], ALU.mult))
            step(v.tensor_tensor(start, start, alive, ALU.add))
            step(v.tensor_scalar(expert, expert, float(NX - 1), None, ALU.min))
            step(v.tensor_copy(route_i[:, 0:MT], expert))
            step(v.tensor_copy(route_i[:, MT:2 * MT], start))
            v.tensor_tensor(route_i[:, 2 * MT:], region8[:, 0:NX], count, ALU.add).then_inc(S["tables_done"], 1)

            dve.sem_inc(S["answer_done"], 1)
            def add_bias(pair, pairs, first):
                for j in range(2):
                    dve.wait_ge(expert_in[j], pairs * 80)
                    if not first:
                        dve.wait_ge(expert_out[j], pair * (16 * HALVES))
                    v.tensor_copy(home[:, j, :], xrow[:, j, :, C])
                    dve.wait_ge(S["expert_y"], pair * 2 + (j + 1))
                    for h in range(HALVES):
                        ins = v.tensor_tensor(ans[:, j, h, :], bank[4 + h][:, 0:C], eb2_t[:, j, :], ALU.add)
                    ins.then_inc(S["answer_done"], 1)

            add_bias(0, 1, True)
            with dve.Fori(1, MT // 2) as pair:
                add_bias(pair, dve.snap(pair + 1), False)

            dve.wait_ge(S["weights_done"], 1)
            step.restart()
            step(v.tensor_scalar(wgt[:, 0, :], wgt[:, 1, :], 1.0, None, ALU.add))
            step(v.reciprocal(wgt[:, 0, :], wgt[:, 0, :]))
            step(v.tensor_tensor(wgt[:, 1, :], wgt[:, 1, :], wgt[:, 0, :], ALU.mult))
            for b in range(NB):
                dve.wait_ge(back_in[b % 2], 32 * (b // 2 + 1))
                for k in range(2):
                    with dve.Fori(0, BATCH) as i:
                        t = i + b * BATCH
                        v.scalar_tensor_tensor(row(acc, t), row(back[:, b % 2, k, :, :], i),
                                               wgt[:, k, :][:, bass.ds(t, 1)], row(acc, t), ALU.mult,
                                               ALU.add).then_inc(S["out_done"], 1)
                    dve.wait_ge(S["out_done"], BATCH * (2 * b + k + 1))

        @block.scalar
        def _(act):
            a = nc.scalar
            with act.Fori(0, NB) as b:
                for i in range(BATCH):
                    act.wait_ge(S["z_transposed"], b * BATCH + (i + 3))
                    act.wait_ge(S["logits_done"], slot_free(b, i))
                    a.activation(zT[:, i % 2, :, :].rearrange("p c q -> p (c q)"),
                                 bank[i % 2][:, 0:C], ACT.Copy).then_inc(S["zT_copied"], 1)
            act.wait_ge(S["logits_ready"], 1)
            a.activation(logit[:, :, 0:QK], logit[:, :, 0:QK], ACT.Exp).then_inc(S["q_exp"], 1)
            with act.Fori(0, NB) as b:
                for i in range(BATCH):
                    act.wait_ge(S["kz_done"], slot_free(b, i))
                    act.wait_ge(S["logits_ready"], 1)
                    a.activation(ek[:, i % 2, :], row(logit, b * BATCH + i)[:, QK:], ACT.Exp).then_inc(S["ek_done"], 1)

            def tile(t, tp1, routed):
                act.wait_ge(S["q_transposed"], tp1)
                a.activation(qT[0:QK, :], bank[1][0:QK, C:C + P], ACT.Copy).then_inc(S["qT_copied"], 1)
                act.wait_ge(S["z2_transposed"], tp1)
                a.activation(z2T[:].rearrange("p c q -> p (c q)"), bank[1][:, 0:C], ACT.Copy).then_inc(S["z2T_copied"], 1)
                for fc in range(FC):
                    if fc == 0:
                        act.wait_ge(S["hidden_a"], tp1)
                    if fc == FC // 2:
                        act.wait_ge(S["hidden_b"], tp1)
                    ins = a.activation(hT[:, fc, :], bank[5 + fc // 4][:, fc % 4 * P:(fc % 4 + 1) * P], ACT.Gelu,
                                       bias=b1f[:, fc:fc + 1])
                    if fc == FC // 2 - 1:
                        ins.then_inc(S["gelu_a"], 1)
                ins.then_inc(S["gelu_b"], 1)
                if routed:
                    gate(t)
                act.wait_ge(S["agg_transposed"], tp1)
                a.activation(aggT[:].rearrange("p c q -> p (c q)"), bank[7][:, 0:C], ACT.Copy).then_inc(S["aggT_copied"], 1)

            def gate(n):
                act.wait_ge(S["z3_transposed"], n)
                a.activation(z3T[:].rearrange("p c q -> p (c q)"), bank[3][:, 0:C], ACT.Copy).then_inc(S["z3T_copied"], 1)

            act.wait_ge(S["attend_copied"], 1)
            tile(0, 1, False)
            with act.Fori(1, T) as t:
                tile(t, act.snap(t + 1), True)
            gate(T)

            act.wait_ge(S["tables_done"], 1)
            a.activation(wgt[:, 1, :], gap[:], ACT.Exp).then_inc(S["weights_done"], 1)

            def copy_rows(n):
                act.wait_ge(S["rows_transposed"], n)
                a.activation(xcol[:].rearrange("p c q -> p (c q)"), bank[6][:], ACT.Copy).then_inc(S["rows_copied"], 1)

            def gelus(j, n):
                for fc in range(FC):
                    if fc % 2 == 0:
                        act.wait_ge(hidden[fc // 2], n)
                    ins = a.activation(hid[:, fc, :], bank[fc // 2][:, fc % 2 * TM:(fc % 2 + 1) * TM], ACT.Gelu,
                                       bias=eb1_t[:, j, fc:fc + 1])
                    if fc % 2:
                        ins.then_inc(gelued[fc // 2], 1)

            copy_rows(1)
            with act.Fori(0, MT // 2 - 1) as pair:
                for j in range(2):
                    n = act.snap(pair * 2 + (j + 1))
                    gelus(j, n)
                    copy_rows(n + 1)
            gelus(0, MT - 1)
            copy_rows(MT)
            gelus(1, MT)

            for b in range(NB):
                act.wait_ge(S["out_done"], 2 * BATCH * (b + 1))
                act.dma_start(out[b * BATCH * P:(b + 1) * BATCH * P, :].rearrange("(t p) c -> p t c", p=P),
                              acc[:, b * BATCH:(b + 1) * BATCH, :]).then_inc(S["out_stored"], 16)
            act.wait_ge(S["out_stored"], 16 * NB)

        @block.tensor
        def _(pe):
            mm, tr = nc.tensor.matmul, nc.tensor.transpose
            W = 2 * QK + C
            pe.wait_ge(S["columns_repeated"], 1)
            mm(bank[0][:, 0:T], ones_f[0:R, :], nbelow[:], start=True, stop=True)
            mm(bank[1][:, 0:1], ones_f[:], wrong[:], start=True, stop=True).then_inc(S["bounds_counted"], 1)
            for i in range(CC):
                for c in range(CC):
                    ins = tr(bank[6 + i][:, c * P:(c + 1) * P], wx[:, c, i * P:(i + 1) * P], ident[:])
            ins.then_inc(S["wx_transposed"], 1)
            pe.wait_ge(S["wxT_copied"], 1)
            pe.wait_ge(S["blocks_loaded"], 16 * 3 * H)
            for c in range(CC):
                for i in range(CC):
                    ins = mm(bank[2 + c][:, 0:W], wxT[:, i, c * P:(c + 1) * P], heads[:, i, :],
                             start=(i == 0), stop=(i == CC - 1))
            ins.then_inc(S["folded"], 1)
            pe.wait_ge(S["fold_copied"], 1)
            for i in range(CC):
                mm(bank[4][:, 0:W], rep[:, 0, i, :], fold[:, i, :], start=(i == 0), stop=False)
            for i in range(CC):
                mm(bank[4][:, 0:W], rep[:, 1, i, :], heads[:, i, :], start=False, stop=(i == CC - 1))
            for fc in range(FC):
                for c in range(CC):
                    ins = mm(bank[5][:, fc:fc + 1], w1[:, c, fc * P:(fc + 1) * P], lncol[:, 3, c:c + 1],
                             start=(c == 0), stop=(c == CC - 1))
            ins.then_inc(S["constants_folded"], 1)

            pe.sem_inc(S["z_transposed"], 2)
            pe.sem_inc(S["logits_done"], 2)
            pe.sem_inc(S["kz_done"], 2)
            with pe.Fori(0, NB) as b:
                for i in range(BATCH + 1):
                    if i < BATCH:
                        pe.wait_ge(S["z_done"], b * BATCH + (i + 1))
                        for c in range(CC):
                            ins = tr(bank[i % 2][:, c * P:(c + 1) * P], z[:, i % 2, c * P:(c + 1) * P], ident[:])
                        ins.then_inc(S["z_transposed"], 1)
                    if i == 1:
                        pe.wait_ge(S["logits_taken"], b + 1)
                    if i > 0:
                        pe.wait_ge(S["zT_copied"], b * BATCH + i)
                        at = (i - 1) * 2 * QK
                        for c in range(CC):
                            ins = mm(bank[6][:, at:at + 2 * QK], zT[:, (i - 1) % 2, c, :], foldg[:, c, 0:2 * QK],
                                     start=(c == 0), stop=(c == CC - 1))
                        ins.then_inc(S["logits_done"], 1)

            pe.wait_ge(S["kmax_done"], 1)
            tr(bank[0][0:QK, 0:P], kmax[:], ident[:]).then_inc(S["kmax_transposed"], 1)
            pe.wait_ge(S["kmax_spread"], 1)
            tr(bank[1][:, 0:QK], kspread[:], ident[0:QK, 0:QK]).then_inc(S["kmax_back"], 1)
            mm(bank[7][0:QK, 0:C + 1], zero[:, 0:QK], zrow[:], start=True, stop=False, skip_group_check=True)
            with pe.Fori(0, NB) as b:
                for i in range(BATCH):
                    pe.wait_ge(S["z_done"], b * BATCH + (T + i + 1))
                    pe.wait_ge(S["ek_done"], b * BATCH + (i + 1))
                    mm(bank[7][0:QK, 0:C + 1], ek[:, i % 2, :], z[:, i % 2, :], start=False, stop=False,
                       skip_group_check=True).then_inc(S["kz_done"], 1)
            pe.wait_ge(S["kz_scaled"], 1)
            for c in range(CC):
                ins = tr(bank[0][:, c * QK:(c + 1) * QK], kz[:, c * P:(c + 1) * P], ident[0:QK, 0:QK])
            ins.then_inc(S["kz_transposed"], 1)
            pe.wait_ge(S["kzT_copied"], 1)
            for c in range(CC):
                ins = mm(bank[1][0:QK, 0:C], kzT[:, c, :], foldg[:, c, 2 * QK:], start=(c == 0), stop=(c == CC - 1))
            ins.then_inc(S["kv_done"], 1)
            pe.wait_ge(S["kv_masked"], 1)
            for c in range(CC):
                ins = tr(bank[2][:, c * QK:(c + 1) * QK], kv[:, c * P:(c + 1) * P], ident[0:QK, 0:QK])
            ins.then_inc(S["kv_transposed"], 1)
            pe.wait_ge(S["kvT_copied"], 1)
            for c in range(CC):
                ins = mm(bank[3][0:QK, 0:C], kvT[:, c, :], wo[:, c, :], start=(c == 0), stop=(c == CC - 1))
            ins.then_inc(S["attend_done"], 1)
            pe.wait_ge(S["attend_copied"], 1)

            pe.wait_ge(S["ring_has_ones"], 1)
            pe.sem_inc(S["groups_free"], R)
            pe.sem_inc(S["onehot_used"], K // 2)

            def visit(t, u, first):
                for k in range(K):
                    if k % 2 == 0:
                        pe.wait_ge(S["onehot_done"], (u + t) * 2 + (k // 2 + 1))
                    ins = mm(bank[0][:, 0:C + 1], onehot[:, k, :],
                             G[:, bass.ds(u % R, 1), k, :].rearrange("p o c -> p (o c)"),
                             start=(first and k == 0), stop=False, skip_group_check=True)
                    if k == 0 and not first:
                        ins.then_inc(S["groups_free"], 1)
                    if k % 2:
                        ins.then_inc(S["onehot_used"], 1)

            def gate(n):
                pe.wait_ge(S["z3_done"], n)
                for c in range(CC):
                    ins = tr(bank[3][:, c * P:(c + 1) * P], sent[:, 0, c * P:(c + 1) * P], ident[:])
                ins.then_inc(S["z3_transposed"], 1)

            def gate_logits(n):
                pe.wait_ge(S["z3T_copied"], n)
                for c in range(CC):
                    ins = mm(bank[3][:, C:C + NX], z3T[:, c, :], wg[:, c, :], start=(c == 0), stop=(c == CC - 1))
                ins.then_inc(S["gates_done"], 1)

            def ranks(n):
                pe.wait_ge(S["picks_done"], n)
                mm(bank[3][:, C + NX:C + 2 * NX], before[:], both[:], start=True, stop=False)
                mm(bank[3][:, C + NX:C + 2 * NX], ones_b[:], taken[:], start=False, stop=True
                   ).then_inc(S["ranks_done"], 1)

            def tile(t, n, routed):
                pe.wait_ge(S["q_staged"], n)
                tr(bank[1][0:QK, C:C + P], q_t[:], ident[:]).then_inc(S["q_transposed"], 1)
                pe.wait_ge(S["qT_copied"], n)
                mm(bank[2][:, 0:C], qT[:], attend[:], start=True, stop=True).then_inc(S["fx_done"], 1)
                lo = pe.value_load(bounds[0:1, bass.ds(t, 1)], min_val=0, max_val=T * NG)
                hi = pe.value_load(bounds[0:1, bass.ds(t + 1, 1)], min_val=0, max_val=T * NG)
                visit(t, lo, True)
                with pe.If(lo < hi):
                    with pe.Fori(lo + 1, hi + 1) as u:
                        visit(t, u, False)
                pe.wait_ge(S["z2_done"], n)
                for c in range(CC):
                    ins = tr(bank[1][:, c * P:(c + 1) * P], z2[:, c * P:(c + 1) * P], ident[:])
                ins.then_inc(S["z2_transposed"], 1)
                pe.wait_ge(S["z2T_copied"], n)
                for fc in range(FC):
                    for c in range(CC):
                        ins = mm(bank[5 + fc // 4][:, fc % 4 * P:(fc % 4 + 1) * P], w1[:, c, fc * P:(fc + 1) * P],
                                 z2T[:, c, :], start=(c == 0), stop=(c == CC - 1))
                    if fc == FC // 2 - 1:
                        ins.then_inc(S["hidden_a"], 1)
                ins.then_inc(S["hidden_b"], 1)
                if routed:
                    gate(t)
                pe.wait_ge(S["agg_done"], n)
                for c in range(CC):
                    ins = tr(bank[7][:, c * P:(c + 1) * P], agg[:, c * P:(c + 1) * P], ident[:])
                ins.then_inc(S["agg_transposed"], 1)
                if routed:
                    gate_logits(t)
                pe.wait_ge(S["aggT_copied"], n)
                for c in range(CC):
                    mm(bank[4][:, 0:C], aggT[:, c, :], gw[:, c, :], start=(c == 0), stop=False)
                for fc in range(FC):
                    if fc == 0:
                        pe.wait_ge(S["gelu_a"], n)
                    if fc == FC // 2:
                        if routed:
                            ranks(t)
                        pe.wait_ge(S["gelu_b"], n)
                    ins = mm(bank[4][:, 0:C], hT[:, fc, :], w2[:, fc, :], start=False, stop=(fc == FC - 1))
                ins.then_inc(S["y_done"], 1)

            tile(0, 1, False)
            with pe.Fori(1, T) as t:
                tile(t, pe.snap(t + 1), True)
            gate(T)
            gate_logits(T)
            ranks(T)
            pe.wait_ge(S["places_done"], T)
            mm(bank[0][:, 0:NX], ones_b[:], taken[:], start=True, stop=True).then_inc(S["picks_counted"], 1)

            def rows_of(j, n):
                pe.wait_ge(expert_in[j], n)
                for c in range(CC):
                    for h in range(HALVES):
                        ins = tr(bank[6][:, c * TM + h * P:c * TM + (h + 1) * P], xrow[:, j, h, c * P:(c + 1) * P],
                                 ident[:])
                ins.then_inc(S["rows_transposed"], 1)

            def up(j, n):
                pe.wait_ge(S["rows_copied"], n)
                for fc in range(FC):
                    for c in range(CC):
                        ins = mm(bank[fc // 2][:, fc % 2 * TM:(fc % 2 + 1) * TM],
                                 ew1[:, j, c, fc * P:(fc + 1) * P], xcol[:, c, :], start=(c == 0), stop=(c == CC - 1))
                    if fc % 2:
                        ins.then_inc(hidden[fc // 2], 1)

            def down(j, n):
                pe.wait_ge(S["answer_done"], n)
                for fc in range(FC):
                    if fc % 2 == 0:
                        pe.wait_ge(gelued[fc // 2], n)
                    for h in range(HALVES):
                        ins = mm(bank[4 + h][:, 0:C], hid[:, fc, h * P:(h + 1) * P], ew2[:, j, fc, :],
                                 start=(fc == 0), stop=(fc == FC - 1))
                ins.then_inc(S["expert_y"], 1)

            rows_of(0, 80)
            with pe.Fori(0, MT // 2 - 1) as pair:
                for j in range(2):
                    n = pe.snap(pair * 2 + (j + 1))
                    up(j, n)
                    rows_of(1 - j, (pair + (1 + j)) * 80)
                    down(j, n)
            up(0, MT - 1)
            rows_of(1, MT // 2 * 80)
            down(0, MT - 1)
            up(1, MT)
            down(1, MT)


def kernel(**inputs):
    import concourse.bacc as _bacc
    from concourse.bass_utils import run_bass_kernel_spmd as _run

    a = {n: np.ascontiguousarray(v) for n, v in inputs.items()}
    n_nodes, width = a["x"].shape
    n_edges = a["src"].shape[0]
    rows, groups = tiles_of(n_nodes) * P, groups_of(n_edges)
    x = np.zeros((rows, width), np.float32)
    x[:n_nodes] = a["x"]
    src = np.zeros(groups * P * K, np.int32)
    src[:n_edges] = a["src"]
    dst = np.full(groups * P * K + 1, NO_NODE, np.int32)
    dst[:n_edges] = a["dst"]
    edges = np.concatenate([src.reshape(groups, P, K), dst[:-1].reshape(groups, P, K)], axis=2)
    given = {"x": x, "edges": np.ascontiguousarray(edges), "dst_line": dst[:-1].copy(), "dst_next": dst[1:].copy()}
    for n in ("gnn_W", "gnn_b", "mix_ln1_g", "mix_ln1_b", "mix_Wx", "mix_bx", "mix_Wq", "mix_Wk", "mix_Wv",
              "mix_Wo", "mix_bo", "mix_ln2_g", "mix_ln2_b", "mix_W1", "mix_b1", "mix_W2", "mix_b2",
              "ffn_Wg", "ffn_bg", "ffn_W1", "ffn_b1", "ffn_W2", "ffn_b2"):
        given[n] = a["L0_" + n]

    nc = _bacc.Bacc("TRN2", target_bir_lowering=False, num_devices=1)
    aps = [nc.dram_tensor(f"in_{n}", v.shape, mybir.dt.from_np(v.dtype), kind="ExternalInput").ap()
           for n, v in given.items()]
    out = nc.dram_tensor("out", (rows, width), F32, kind="ExternalOutput").ap()
    build(nc, n_nodes, *aps, out)
    r = _run(nc, [{f"in_{n}": v for n, v in given.items()}], core_ids=[0])
    return r.results[0]["out"][:n_nodes]
```
